# Optimizing a Trainium2 kernel written in Bass

```python
import numpy as np
import jax
import jax.numpy as jnp

def _softmax(x, axis=-1):
    return jax.nn.softmax(x, axis=axis)

def _gelu(x):
    return jax.nn.gelu(x, approximate=True)

def _silu(x):
    return jax.nn.silu(x)

def _sigmoid(x):
    return jax.nn.sigmoid(x)

def _layernorm(x, axis=-1, eps=1e-05):
    m = jnp.mean(x, axis=axis, keepdims=True)
    v = jnp.var(x, axis=axis, keepdims=True)
    return (x - m) / jnp.sqrt(v + eps)

def _scatter_add(tgt, idx, src, axis=0):
    return tgt.at[idx].add(src)

def _segment_sum(src, seg, n):
    return jax.ops.segment_sum(src, seg, n)
kernel_name = 'mk_adaln_d1_jaxref_r8_8e65b1'

def setup_inputs(seed: int=0):
    np.random.seed(seed)
    _w = jnp.asarray

    def _L0_attn_setup():
        import jax, jax.numpy as jnp
        import numpy as np
        B, N, D, H = (4, 512, 128, 16)
        HD = D // H
        EPS_NORM = 1e-12
        EPS_LN = 1e-05

        def _silu(x):
            return x * jax.nn.sigmoid(x)

        def _simple_gla(q, k, v, f):
            qT = jnp.moveaxis(q, 1, 0)
            kT = jnp.moveaxis(k, 1, 0)
            vT = jnp.moveaxis(v, 1, 0)
            fT = jnp.moveaxis(f, 1, 0)

            def step(S, inp):
                qt, kt, vt, ft = inp
                S = jnp.exp(ft)[..., None, None] * S + kt[..., :, None] * vt[..., None, :]
                o = jnp.einsum('bhk,bhkv->bhv', qt, S)
                return (S, o)
            S0 = jnp.zeros((q.shape[0], q.shape[2], q.shape[3], v.shape[3]), q.dtype)
            _, o = jax.lax.scan(step, S0, (qT, kT, vT, fT))
            return jnp.moveaxis(o, 0, 1)
        key = jax.random.key(seed)
        ks = jax.random.split(key, 9)
        s = 0.02
        return {'x': jax.random.normal(ks[0], (B, N, D), jnp.float32), 'Wq': jax.random.normal(ks[1], (D, D), jnp.float32) * s, 'Wk': jax.random.normal(ks[2], (D, D), jnp.float32) * s, 'Wv': jax.random.normal(ks[3], (D, D), jnp.float32) * s, 'Wf': jax.random.normal(ks[4], (H, D), jnp.float32) * s, 'Wg1': jax.random.normal(ks[5], (HD, D), jnp.float32) * s, 'Wg2': jax.random.normal(ks[6], (D, HD), jnp.float32) * s, 'ln_w': jnp.ones((D,), jnp.float32), 'Wo': jax.random.normal(ks[7], (D, D), jnp.float32) * s}
    _L0_attn_in = _L0_attn_setup()

    def _L0_ffn_setup():
        import jax, jax.numpy as jnp
        import numpy as np
        B, S, DIM = (2, 256, 128)
        HID = 256
        E, NSH, TOPK = (8, 2, 2)

        def _ffn(x, w1, w2, w3):
            return jax.nn.silu(x @ w1.T) * (x @ w3.T) @ w2.T
        key = jax.random.key(seed)
        ks = jax.random.split(key, 8)
        sc = 0.02
        return {'x': jax.random.normal(ks[0], (B, S, DIM), jnp.float32), 'router_w': jax.random.normal(ks[1], (E, DIM), jnp.float32) * sc, 'expert_bias': jnp.zeros((E,), jnp.float32), 'w1': jax.random.normal(ks[2], (E, HID, DIM), jnp.float32) * sc, 'w3': jax.random.normal(ks[3], (E, HID, DIM), jnp.float32) * sc, 'w2': jax.random.normal(ks[4], (E, DIM, HID), jnp.float32) * sc, 'sw1': jax.random.normal(ks[5], (NSH, HID, DIM), jnp.float32) * sc, 'sw3': jax.random.normal(ks[6], (NSH, HID, DIM), jnp.float32) * sc, 'sw2': jax.random.normal(ks[7], (NSH, DIM, HID), jnp.float32) * sc}
    _L0_ffn_in = _L0_ffn_setup()
    _L0_c = _w((lambda *s: np.random.randn(*s).astype(np.float32) * 0.05)(4, 128))
    _L0_wmod = _w((lambda *s: np.random.randn(*s).astype(np.float32) * 0.05)(128, 6 * 128) * 128 ** (-0.5))
    _d = {'L0_attn_x': _L0_attn_in['x'], 'L0_attn_Wq': _L0_attn_in['Wq'], 'L0_attn_Wk': _L0_attn_in['Wk'], 'L0_attn_Wv': _L0_attn_in['Wv'], 'L0_attn_Wf': _L0_attn_in['Wf'], 'L0_attn_Wg1': _L0_attn_in['Wg1'], 'L0_attn_Wg2': _L0_attn_in['Wg2'], 'L0_attn_ln_w': _L0_attn_in['ln_w'], 'L0_attn_Wo': _L0_attn_in['Wo'], 'L0_ffn_router_w': _L0_ffn_in['router_w'], 'L0_ffn_expert_bias': _L0_ffn_in['expert_bias'], 'L0_ffn_w1': _L0_ffn_in['w1'], 'L0_ffn_w3': _L0_ffn_in['w3'], 'L0_ffn_w2': _L0_ffn_in['w2'], 'L0_ffn_sw1': _L0_ffn_in['sw1'], 'L0_ffn_sw3': _L0_ffn_in['sw3'], 'L0_ffn_sw2': _L0_ffn_in['sw2'], 'L0_c': _L0_c, 'L0_wmod': _L0_wmod}
    _x0 = _d['L0_attn_x']
    _d['L0_attn_x'] = jax.random.normal(jax.random.fold_in(jax.random.key(seed), 1), (4, 1024, 128), dtype=_x0.dtype)
    del _x0
    return _d

def reference(L0_attn_x, L0_attn_Wq, L0_attn_Wk, L0_attn_Wv, L0_attn_Wf, L0_attn_Wg1, L0_attn_Wg2, L0_attn_ln_w, L0_attn_Wo, L0_ffn_router_w, L0_ffn_expert_bias, L0_ffn_w1, L0_ffn_w3, L0_ffn_w2, L0_ffn_sw1, L0_ffn_sw3, L0_ffn_sw2, L0_c, L0_wmod):

    def _L0_attn_ref(x, Wq, Wk, Wv, Wf, Wg1, Wg2, ln_w, Wo):
        import jax, jax.numpy as jnp
        import numpy as np
        B, N, D, H = (4, 512, 128, 16)
        HD = D // H
        EPS_NORM = 1e-12
        EPS_LN = 1e-05

        def _silu(x):
            return x * jax.nn.sigmoid(x)

        def _simple_gla(q, k, v, f):
            qT = jnp.moveaxis(q, 1, 0)
            kT = jnp.moveaxis(k, 1, 0)
            vT = jnp.moveaxis(v, 1, 0)
            fT = jnp.moveaxis(f, 1, 0)

            def step(S, inp):
                qt, kt, vt, ft = inp
                S = jnp.exp(ft)[..., None, None] * S + kt[..., :, None] * vt[..., None, :]
                o = jnp.einsum('bhk,bhkv->bhv', qt, S)
                return (S, o)
            S0 = jnp.zeros((q.shape[0], q.shape[2], q.shape[3], v.shape[3]), q.dtype)
            _, o = jax.lax.scan(step, S0, (qT, kT, vT, fT))
            return jnp.moveaxis(o, 0, 1)
        b, n, d = x.shape
        q = _silu(x @ Wq.T).reshape(b, n, H, HD)
        k = _silu(x @ Wk.T).reshape(b, n, H, HD)
        v = _silu(x @ Wv.T).reshape(b, n, H, HD)
        f = jax.nn.log_sigmoid(x @ Wf.T)
        k = k / jnp.maximum(jnp.linalg.norm(k, axis=-1, keepdims=True), EPS_NORM)
        o = _simple_gla(q, k, v, f).reshape(b, n, d)
        gate = jax.nn.sigmoid(x @ Wg1.T @ Wg2.T)
        o = o * gate
        mu = jnp.mean(o, axis=-1, keepdims=True)
        xc = o - mu
        var = jnp.mean(xc * xc, axis=-1, keepdims=True)
        o = xc / jnp.sqrt(var + EPS_LN) * ln_w
        return o @ Wo.T

    def _L0_ffn_ref(x, router_w, expert_bias, w1, w3, w2, sw1, sw3, sw2):
        import jax, jax.numpy as jnp
        import numpy as np
        B, S, DIM = (2, 256, 128)
        HID = 256
        E, NSH, TOPK = (8, 2, 2)

        def _ffn(x, w1, w2, w3):
            return jax.nn.silu(x @ w1.T) * (x @ w3.T) @ w2.T
        bs, sl, d = x.shape
        xf = x.reshape(-1, d)
        shared = jnp.zeros_like(xf)
        for i in range(sw1.shape[0]):
            shared = shared + _ffn(xf, sw1[i], sw2[i], sw3[i])
        logits = xf @ router_w.T + expert_bias
        rw, sel = jax.lax.top_k(logits, TOPK)
        rw = jax.nn.softmax(rw.astype(jnp.float32), axis=-1).astype(x.dtype)
        onehot = jax.nn.one_hot(sel, E, dtype=x.dtype)
        combine = jnp.einsum('tk,tke->te', rw, onehot)

        def body(acc, ew):
            e1, e3, e2, cw = ew
            acc = acc + cw[:, None] * _ffn(xf, e1, e2, e3)
            return (acc, None)
        out, _ = jax.lax.scan(body, jnp.zeros_like(xf), (w1, w3, w2, combine.T))
        out = out + shared
        return out.reshape(bs, sl, -1)
    x = L0_attn_x
    mod = (_silu(L0_c) @ L0_wmod).reshape(L0_c.shape[0], 6, 1, -1)
    sa, ca, ga, sb, cb, gb = (mod[:, 0], mod[:, 1], mod[:, 2], mod[:, 3], mod[:, 4], mod[:, 5])
    ga = (2 * (ga >= 0) - 1) * jnp.maximum(jnp.abs(ga), 0.25)
    gb = (2 * (gb >= 0) - 1) * jnp.maximum(jnp.abs(gb), 0.25)
    h = _layernorm(x, axis=-1) * (1 + ca) + sa
    x = x + ga * _L0_attn_ref(h, L0_attn_Wq, L0_attn_Wk, L0_attn_Wv, L0_attn_Wf, L0_attn_Wg1, L0_attn_Wg2, L0_attn_ln_w, L0_attn_Wo)
    h = _layernorm(x, axis=-1) * (1 + cb) + sb
    x = x + gb * _L0_ffn_ref(h, L0_ffn_router_w, L0_ffn_expert_bias, L0_ffn_w1, L0_ffn_w3, L0_ffn_w2, L0_ffn_sw1, L0_ffn_sw3, L0_ffn_sw2)
    return x

_drawn_inputs = setup_inputs


def setup_inputs(seed=0):
    import zlib

    import numpy as np

    out = dict(_drawn_inputs(seed))
    spreads = {'L0_attn_ln_w': (1.0, 0.6), 'L0_ffn_expert_bias': (0.0, 0.8)}
    factors = {'L0_attn_Wf': 8.0,
     'L0_attn_Wg1': 8.0,
     'L0_attn_Wg2': 8.0,
     'L0_ffn_router_w': 8.0,
     'L0_ffn_w1': 8.0,
     'L0_ffn_w3': 8.0,
     'L0_ffn_w2': 8.0,
     'L0_ffn_sw1': 8.0,
     'L0_ffn_sw3': 8.0,
     'L0_ffn_sw2': 8.0}
    for name, (base, spread) in spreads.items():
        noise = np.random.default_rng([zlib.crc32(name.encode()), seed]).standard_normal(out[name].shape)
        drawn = base * np.exp(spread * noise) if base else spread * noise
        out[name] = jnp.asarray(drawn.astype(out[name].dtype))
    for name, factor in factors.items():
        out[name] = (out[name] * factor).astype(out[name].dtype)
    return out
```

```python
from contextlib import ExitStack

import concourse.bass as bass
from concourse import mybir

ALU = mybir.AluOpType
ACT = mybir.ActivationFunctionType
AX = mybir.AxisListType
F32 = mybir.dt.float32
F32R = mybir.dt.float32r
I32 = mybir.dt.int32

P = 128
TB = 512
NT = TB // P
RSQRT_SEED = 0x5F3759DF


def wait(eng, sem, value):
    if isinstance(value, int) and value <= 0:
        return
    eng.wait_ge(sem, value)


class Chain:

    def __init__(self, eng, sem, before):
        self.eng, self.sem, self.before, self.n = eng, sem, before, 0

    def __call__(self, ins):
        self.n += 1
        ins.then_inc(self.sem, 1)
        self.eng.wait_ge(self.sem, self.before + self.n)


def rsqrt(dve, link, y, x, t):
    link(dve.tensor_scalar(t.bitcast(I32), x.bitcast(I32), 1, None, ALU.logical_shift_right))
    link(dve.tensor_scalar(y.bitcast(I32), t.bitcast(I32), -1, RSQRT_SEED, ALU.mult, ALU.add))
    link(dve.tensor_tensor(t, x, y, ALU.mult))
    link(dve.scalar_tensor_tensor(t, t, -0.5, y, ALU.mult, ALU.mult))
    link(dve.scalar_tensor_tensor(y, t, 1.5, y, ALU.add, ALU.mult))
    root = 0.375 ** 0.5
    link(dve.scalar_tensor_tensor(t, x, root, y, ALU.mult, ALU.mult))
    link(dve.tensor_tensor(t, t, y, ALU.mult))
    link(dve.scalar_tensor_tensor(t, t, -1.25 / root, t, ALU.add, ALU.mult))
    link(dve.scalar_tensor_tensor(y, t, 1.875, y, ALU.add, ALU.mult))


RSQRT_STEPS = 9
U = 12
RING = 4
V = 4
AHEAD, BEHIND_T, BEHIND_D = 2, 2, 3


def build(nc, x, cmod, attw, wg12, w13T, w2T, bias, consts, ids, tiles, pads, H, out):
    B, N, D = x.shape
    HD = D // H
    NEXP = bias.shape[0]
    NFF = w13T.shape[1]
    NSH = NFF - NEXP
    HID = w13T.shape[2] // 2
    NB = B * N // TB
    BPB = N // TB
    NC = HID // P
    NF1 = NSH * NC
    NTOK = B * N
    REG = NTOK + P
    NTILE = tiles.shape[1] - NEXP
    TURNS = NTILE // U
    ROW = P + 1
    assert D == P and NC == 2 and NEXP == 8 and NSH == 2 and HD == 8 and N % TB == 0
    assert NTILE % U == 0 and U % RING == 0 and NTILE >= 2 * NTOK // P + NEXP - 1 and TURNS >= 3

    h_dram = nc.dram_tensor("h_dram", [NEXP * REG + (NTILE - 2 * NTOK // P) * P, ROW], F32).ap()
    y_dram = nc.dram_tensor("y_dram", [2 * NTOK + pads.shape[0] * P, P], F32).ap()
    y_tiles = y_dram[0:2 * NTOK].rearrange("(n p) d -> p n d", p=P)

    x_tiles = x.rearrange("b (k t p) d -> (b k) p t d", t=NT, p=P)
    out_tiles = out.rearrange("b (k t p) d -> p (b k t) d", t=NT, p=P)

    with ExitStack() as ctx:
        def sb(name, shape, dt=F32):
            return ctx.enter_context(nc.sbuf_tensor(name, shape, dt))

        def sem(name):
            return ctx.enter_context(nc.semaphore(name))

        def parts(whole, *widths):
            ends = [sum(widths[:n + 1]) for n in range(len(widths))]
            return [whole[:, e - w:e] for e, w in zip(ends, widths)]

        consts_sb = sb("consts_sb", list(consts.shape))
        ident, head_ones, block_diag, center, before, ones, mean_col, rank, keep, region = \
            parts(consts_sb, P, H, P, P, P, P, 1, NEXP, NB, NEXP)
        ids_sb = sb("ids_sb", [P, 2, NB * NT], I32)
        tiles_sb = sb("tiles_sb", [1, NTILE + NEXP])
        tile_no, one_row = tiles_sb[:, 0:NTILE], tiles_sb[:, NTILE:NTILE + NEXP]
        spread_v = sb("spread_v", [P, HD, P], F32R)
        gather_v = sb("gather_v", [P, HD, P])
        cmod_sb = sb("cmod_sb", [P, B + 6 * P])
        c_sb, wmod_sb = parts(cmod_sb, B, 6 * P)
        sc = sb("sc", [P, B])
        sc_wide = sb("sc_wide", [P, B, P])
        shift1 = sb("shift1", [P, NB])
        scale1 = sb("scale1", [P, NB])
        shift2 = sb("shift2", [P, NB])
        scale2 = sb("scale2", [P, NB])
        gain_b = sb("gain_b", [P, NB, P])
        scale2_row = sb("scale2_row", [P, NB, P])
        shift2_row = sb("shift2_row", [P, NB, P])
        watt = sb("watt", [P, 5, P])
        watt_hi = sb("watt_hi", [P, 5, P], F32R)
        watt_lo = sb("watt_lo", [P, 5, P], F32R)
        attw_sb = sb("attw_sb", [P, 4 * P + H + 1 + NEXP])
        wqkv_sb, wf_sb, wo_sb, lnw_sb, rw_sb = parts(attw_sb, 3 * P, H, P, 1, NEXP)
        wg_sb = sb("wg_sb", [HD, 2 * P])
        wg1_sb, wg2_sb = parts(wg_sb, P, P)
        wo_ln = sb("wo_ln", [P, P])
        wo_blk = sb("wo_blk", [P, NB, P])
        w13_hi = sb("w13_hi", [P, NFF, NC * 2 * P], F32R)
        w13_lo = sb("w13_lo", [P, NFF, NC * 2 * P], F32R)
        w2_sb = sb("w2_sb", [P, NFF, NC, P])
        bias_sb = sb("bias_sb", [P, NEXP])

        xall = sb("xall", [P, NB * NT, P])
        bn = sb("bn", [P, NB * NT, 6])
        mv = sb("mv", [P, NB * NT, 2])
        var1 = sb("var1", [P, NB * NT])
        rstd1 = sb("rstd1", [P, NB * NT])
        nmr1 = sb("nmr1", [P, NB * NT])
        tmp1 = sb("tmp1", [P, NB * NT])

        xn1 = sb("xn1", [P, NT, P])
        hT = sb("hT", [P, TB])
        hT_hi = sb("hT_hi", [P, TB], F32R)
        hT_lo = sb("hT_lo", [P, TB], F32R)
        qT = sb("qT", [P, TB])
        kT = sb("kT", [P, TB])
        vT = sb("vT", [P, TB])
        vT_hi = sb("vT_hi", [P, TB], F32R)
        vT_lo = sb("vT_lo", [P, TB], F32R)
        decay = sb("decay", [P, TB])
        gate = sb("gate", [P, TB])
        ksq = sb("ksq", [P, TB])
        sq = sb("sq", [P, NT * H + NT])
        rsq = sb("rsq", [P, NT * H + NT])
        rtmp = sb("rtmp", [P, NT * H + NT])
        n2, ovar = parts(sq, NT * H, NT)
        rn, orstd = parts(rsq, NT * H, NT)
        rn_wide = sb("rn_wide", [P, NT, H, HD])
        khat = sb("khat", [P, TB])
        upd = sb("upd", [P, 3, TB])
        S = sb("S", [P, HD, TB])
        S0 = sb("S0", [P, HD])
        qS = sb("qS", [P, 2, TB])
        og = sb("og", [P, TB])
        oc = sb("oc", [P, TB])
        oc_sq = sb("oc_sq", [P, TB])

        carrier = sb("carrier", [P, 5])
        bn2 = sb("bn2", [P, NT, 6])
        mv2 = sb("mv2", [P, NT, 2])
        var2 = sb("var2", [P, NT])
        rstd2 = sb("rstd2", [P, NT])
        nmr2 = sb("nmr2", [P, NT])
        tmp2 = sb("tmp2", [P, NT])
        xn2 = sb("xn2", [P, NT, P])
        h2 = sb("h2", [P, 2, NT, ROW])
        h2T_hi = sb("h2T_hi", [P, TB], F32R)
        h2T_lo = sb("h2T_lo", [P, TB], F32R)
        lg = sb("lg", [P, NT, NEXP])
        eq = sb("eq", [P, 2, NT, NEXP])
        hot = sb("hot", [P, 2, NT, NEXP])
        both = sb("both", [P, NT, NEXP])
        earlier = sb("earlier", [P, NT + 1, NEXP])
        top = sb("top", [P, NT, 8])
        r = sb("r", [P, 2, NT])
        dif = sb("dif", [P, NT])
        wt = sb("wt", [P, 2, NB * NT])
        tanh_d = sb("tanh_d", [P, NT])
        place = sb("place", [P, NT, NEXP])
        chosen = sb("chosen", [P, 2, NT, NEXP])
        target = sb("target", [P, 2, NT])
        target_i = sb("target_i", [P, 2, NT], I32)
        work = sb("work", [P, NFF * TB])
        w13 = work[:, :].rearrange("p (e n) -> p e n", n=TB)
        G, silu, shared, h2T = parts(work, NF1 * TB, NC * TB, TB, TB)
        G = G.rearrange("p (c n) -> p c n", n=TB)
        silu = silu.rearrange("p (c n) -> p c n", n=TB)
        shared = shared.rearrange("p (t n) -> p t n", n=P)
        gain_a, gain_b1, gsign, gabs = (a[:, :].rearrange("p (b n) -> p b n", n=P) for a in
                                       (og, oc, oc_sq, xn2[:, :, :].rearrange("p t n -> p (t n)")))

        counts = sb("counts", [1, NEXP])
        ntiles_i = sb("ntiles_i", [1, NEXP], I32)
        ntiles = sb("ntiles", [1, NEXP])
        last = sb("last", [1, NEXP])
        jump = sb("jump", [1, NEXP])
        pad_row = sb("pad_row", [1, NEXP], I32)
        past, skip = (a[0:1, :, :].rearrange("p a n -> p (a n)")[:, 0:NTILE * NEXP].rearrange("p (j e) -> p j e", e=NEXP)
                      for a in (upd, qS))
        tile_sum = sb("tile_sum", [1, 2, NTILE])
        tile_row = sb("tile_row", [1, NTILE], I32)
        tile_expert = sb("tile_expert", [1, NTILE + BEHIND_D], I32)

        rows, y_sb, t_silu = (a.rearrange("p (u n) -> p u n", n=n) for a, n in zip(
            parts(S[:, :, :].rearrange("p v n -> p (v n)"), U * ROW, U * P, 2 * HID), (ROW, P, HID)))
        t_G = upd[:, 0:2, :].rearrange("p a (r n) -> p (a r) n", n=HID)
        t_GT = qS[:, :, :].rearrange("p a (r n) -> p (a r) n", n=HID)
        t_hi, t_lo = (a[:, :].rearrange("p (r n) -> p r n", n=P) for a in (vT_hi, vT_lo))

        y_in = S[:, :, :].rearrange("p (k u) n -> p u k n", u=V)
        total, res = (a.rearrange("p (u n) -> p u n", n=TB) for a in parts(work, V * TB, V * TB))

        ff = [ctx.enter_context(nc.psum_tensor(f"ff{n}", [P, TB], F32)) for n in range(4)]
        ybank = ctx.enter_context(nc.psum_tensor("ybank", [P, TB], F32))
        at = [ctx.enter_context(nc.psum_tensor(f"at{n}", [P, TB], F32)) for n in range(2)]
        obank = ctx.enter_context(nc.psum_tensor("obank", [P, TB], F32))

        ld = {n: sem("ld_" + n) for n in ("consts", "mod", "attw", "x0", "x1", "xrest", "w13", "w2", "table")}
        s_set = sem("s_set")
        s_sc = sem("s_sc")
        s_scw = sem("s_scw")
        s_mod = sem("s_mod")
        s_rows = sem("s_rows")
        s_gain_b = sem("s_gain_b")
        s_watt = sem("s_watt")
        s_watt_hi = sem("s_watt_hi")
        s_watt_lo = sem("s_watt_lo")
        s_gains = sem("s_gains")
        s_row2 = sem("s_row2")
        s_ready = sem("s_ready")
        s_w13_hi = sem("s_w13_hi")
        s_w13_lo = sem("s_w13_lo")
        s_st1 = sem("s_st1")
        s_xn1 = sem("s_xn1")
        s_t1 = sem("s_t1")
        s_hT = sem("s_hT")
        s_hT_hi = sem("s_hT_hi")
        s_hT_lo = sem("s_hT_lo")
        s_proj = sem("s_proj")
        s_act = sem("s_act")
        s_ksq = sem("s_ksq")
        s_v_hi = sem("s_v_hi")
        s_v_lo = sem("s_v_lo")
        s_decay = sem("s_decay")
        s_gate = sem("s_gate")
        s_n2 = sem("s_n2")
        s_norm = sem("s_norm")
        s_rnw = sem("s_rnw")
        s_rnT = sem("s_rnT")
        s_khat = sem("s_khat")
        s_S0 = sem("s_S0")
        s_vb = sem("s_vb")
        s_upd = sem("s_upd")
        s_scan = sem("s_scan")
        s_qS = sem("s_qS")
        s_q7 = sem("s_q7")
        s_red = sem("s_red")
        s_og = sem("s_og")
        s_ctr = sem("s_ctr")
        s_oc = sem("s_oc")
        s_sq = sem("s_sq")
        s_out = sem("s_out")
        s_var = sem("s_var")
        s_varc = sem("s_varc")
        s_ln = sem("s_ln")
        s_x2 = sem("s_x2")
        s_st = sem("s_st")
        s_st2 = sem("s_st2")
        s_xn2 = sem("s_xn2")
        s_mod2 = sem("s_mod2")
        s_copy2 = sem("s_copy2")
        s_ids = sem("s_ids")
        s_t2 = sem("s_t2")
        s_h2T = sem("s_h2T")
        s_h2_hi = sem("s_h2_hi")
        s_h2_lo = sem("s_h2_lo")
        s_logit = sem("s_logit")
        s_rt = sem("s_rt")
        s_dif = sem("s_dif")
        s_tanh = sem("s_tanh")
        s_wt = sem("s_wt")
        s_early = sem("s_early")
        s_pos = sem("s_pos")
        s_tgt = sem("s_tgt")
        s_target = sem("s_target")
        s_car = sem("s_car")
        s_scatter = sem("s_scatter")
        s_f1 = sem("s_f1")
        s_silu = sem("s_silu")
        s_G = sem("s_G")
        s_f2 = sem("s_f2")
        s_shared = sem("s_shared")
        s_shg = sem("s_shg")
        s_xsh = sem("s_xsh")
        s_total = sem("s_total")
        s_tab = sem("s_tab")
        s_prow = sem("s_prow")
        s_table = sem("s_table")
        s_pad = sem("s_pad")
        s_trow = [sem(f"s_trow{u}") for u in range(U)]
        s_yrow = [sem(f"s_yrow{u}") for u in range(U)]
        s_tr = sem("s_tr")
        s_thi = sem("s_thi")
        s_tlo = sem("s_tlo")
        s_tf1 = sem("s_tf1")
        s_tsilu = sem("s_tsilu")
        s_tG = sem("s_tG")
        s_tGt = sem("s_tGt")
        s_tGT = sem("s_tGT")
        s_tf2 = sem("s_tf2")
        s_ty = sem("s_ty")
        s_tcar = sem("s_tcar")
        s_yin = [sem(f"s_yin{u}") for u in range(V)]
        s_part = sem("s_part")
        s_sum = sem("s_sum")
        s_fin = sem("s_fin")
        s_out3 = sem("s_out3")
        s_store = [sem(f"s_store{u}") for u in range(V)]

        TGT_STEPS = 4
        RT_STEPS = 9

        block = ctx.enter_context(nc.Block())

        def blocks(eng, body):
            body(0, False, True, True)
            body(1, True, True, True)
            with eng.Fori(2, NB - 1) as i:
                body(i, True, True, True)
            body(NB - 1, True, True, False)
            body(NB, True, False, False)

        ORDER = (1, 3, 2, 4, 0)

        def bank_of(b, n):
            if isinstance(b, int) and b == 0:
                return at[(n + 1) % 2]
            return ff[(0, 2, 0, 3, 2)[n]]

        def norm_bank(b):
            return ff[0] if isinstance(b, int) and b == 0 else ff[1]

        def turns(eng, body):
            body(0, True, False)
            with eng.Fori(1, TURNS - 1) as q:
                body(q, False, False)
            body(TURNS - 1, False, True)

        def step(f, q, u, off, first, last):
            turn, slot = divmod(u + off, U)
            if not (first and turn < 0) and not (last and turn > 0):
                f(q + turn if turn else q, slot)

        def groups(eng, body):
            body(0)
            with eng.Fori(1, NB // V) as m:
                body(m)

        @block.sync
        def _(sp):
            sp.dma_start(cmod_sb[:, :], cmod).then_inc(ld["mod"], 16)
            sp.dma_start(xall[:, 0:NT, :], x_tiles[0]).then_inc(ld["x0"], 16)
            sp.dma_start(attw_sb[:, :], attw).then_inc(ld["attw"], 16)
            sp.dma_start(wg_sb[:, :], wg12).then_inc(ld["attw"], 16)
            sp.dma_start(consts_sb[:, :], consts).then_inc(ld["consts"], 16)
            sp.dma_start(bias_sb[:, :], bias.partition_broadcast(P)).then_inc(ld["attw"], 16)
            sp.dma_start(xall[:, NT:2 * NT, :], x_tiles[1]).then_inc(ld["x1"], 16)
            for b in range(2, NB):
                sp.dma_start(xall[:, b * NT:(b + 1) * NT, :], x_tiles[b]).then_inc(ld["xrest"], 16)
            sp.dma_start(ids_sb[:, :, :], ids).then_inc(ld["table"], 16)
            sp.dma_start(tiles_sb[:, :], tiles).then_inc(ld["table"], 16)
            sp.dma_start(w13, w13T).then_inc(ld["w13"], 16)
            sp.dma_start(w2_sb[:, :, :, :], w2T).then_inc(ld["w2"], 16)
            sp.dma_start(h_dram[NEXP * REG:, :].rearrange("(n p) w -> n p w", p=P),
                         pads[NEXP:, :, :]).then_inc(s_pad, 16)
            sp.wait_ge(s_prow, 1)
            for e in range(NEXP):
                r = sp.value_load(pad_row[0:1, e:e + 1], min_val=e * REG, max_val=e * REG + NTOK)
                sp.dma_start(h_dram[bass.ds(r, P), :], pads[e, :, :]).then_inc(s_pad, 16)
            sp.wait_ge(s_table, 1)
            sp.wait_ge(s_pad, 16 * (NEXP + 1))
            sp.wait_ge(s_scatter, 16 * 2 * NT * NB)

            def body(q, first, last):
                for u in range(U):
                    r = sp.value_load(tile_row[0:1, bass.ds(q * U + u, 1)], min_val=0, max_val=h_dram.shape[0] - P)
                    wait(sp, s_yrow[u], 16 * q)
                    sp.dma_start(rows[:, u, :], h_dram[bass.ds(r, P), :]).then_inc(s_trow[u], 16)

            turns(sp, body)
            for u in range(U):
                sp.wait_ge(s_yrow[u], 16 * TURNS)

            def load(m, u):
                wait(sp, s_sum, V * m + u + 1 - V)
                for k in range(2):
                    sp.dma_start(y_in[:, u, k, :].rearrange("p (t n) -> p t n", n=P),
                                 y_tiles[:, bass.ds(k * NB * NT + (V * m + u) * NT, NT), :]).then_inc(s_yin[u], 16)

            def store(m, u):
                wait(sp, s_out3, V * m + u + 1)
                sp.dma_start(out_tiles[:, bass.ds((V * m + u) * NT, NT), :],
                             res[:, u, :].rearrange("p (t n) -> p t n", n=P)).then_inc(s_store[u], 16)

            for u in range(V):
                load(0, u)
            with sp.Fori(1, NB // V) as m:
                for u in range(V):
                    load(m, u)
                    store(m - 1, u)
            for u in range(V):
                store(NB // V - 1, u)
            for u in range(V):
                sp.wait_ge(s_store[u], 16 * (NB // V))

        LD = {"consts": 16, "mod": 16, "attw": 3 * 16, "x0": 16, "x1": 16, "xrest": (NB - 2) * 16, "w13": 16, "w2": 16, "table": 32}

        @block.tensor
        def _(pe):
            def split3(dst, w_hi, w_lo, h_hi, h_lo):
                pe.matmul(dst, w_hi, h_hi, start=True, stop=False)
                pe.matmul(dst, w_hi, h_lo, start=False, stop=False)
                return pe.matmul(dst, w_lo, h_hi, start=False, stop=True)

            pe.wait_ge(ld["mod"], LD["mod"])
            pe.wait_ge(ld["attw"], LD["attw"])
            pe.wait_ge(s_scw, 1)
            for n, j in enumerate((0, 1, 3, 4)):
                pe.matmul(ff[0][:, n * B:(n + 1) * B], wmod_sb[:, j * P:(j + 1) * P], sc[:, :], start=True, stop=True)
            pe.matmul(ff[3][:, 0:P], wg1_sb[:, :], wg2_sb[:, :], start=True, stop=True).then_inc(s_mod, 1)

            def by_row(bank, j):
                for b in range(B):
                    ins = pe.matmul(bank[:, b * P:(b + 1) * P], sc_wide[:, b, :], wmod_sb[:, j * P:(j + 1) * P],
                                    start=True, stop=True)
                ins.then_inc(s_rows, 1)

            by_row(ff[1], 2)
            pe.wait_ge(ld["consts"], LD["consts"])

            def transpose_x1(b):
                wait(pe, s_xn1, b + 1)
                bank = at[0] if isinstance(b, int) and b == 0 else obank
                if isinstance(b, int) and b == 1:
                    pe.wait_ge(s_row2, 1)
                elif isinstance(b, int) and b == 0:
                    pass
                else:
                    wait(pe, s_og, b - 1)
                for t in range(NT):
                    ins = pe.transpose(bank[:, t * P:(t + 1) * P], xn1[:, t, :], ident[:, :])
                ins.then_inc(s_t1, 1)

            transpose_x1(0)
            by_row(ff[2], 5)
            pe.wait_ge(s_watt_hi, 1)
            pe.wait_ge(s_watt_lo, 1)

            def keep_clock(b, count):
                wait(pe, s_og, b)
                for _ in range(count):
                    pe.matmul(obank[:, :], spread_v[:, 0, :], spread_v[:, 0:NT, :].rearrange("p v n -> p (v n)"),
                              start=True, stop=True)

            def project(b, n, f=None):
                if n == 0:
                    wait(pe, s_hT_hi, b + 1)
                    wait(pe, s_hT_lo, b + 1)
                    if isinstance(b, int) and b == 1:
                        pe.wait_ge(s_norm, 1)
                    if f is not None:
                        wait(pe, s_G, NF1 * f + NF1 - 1)
                elif n == 1:
                    if f is not None:
                        wait(pe, s_G, NF1 * f + NF1)
                    elif isinstance(b, int) and b == 0:
                        pe.wait_ge(s_hT, 1)
                    else:
                        pe.wait_ge(s_gains, 1)
                else:
                    wait(pe, s_act, 5 * b + n - 1)
                w = ORDER[n]
                split3(bank_of(b, n)[:, :], watt_hi[:, w, :], watt_lo[:, w, :], hT_hi[:, :], hT_lo[:, :]) \
                    .then_inc(s_proj, 1)

            def k_norms(b):
                wait(pe, s_ksq, b + 1)
                for t in range(NT):
                    ins = pe.matmul(norm_bank(b)[:, t * H:(t + 1) * H], ksq[:, t * P:(t + 1) * P], head_ones[:, :],
                                    start=True, stop=True)
                ins.then_inc(s_n2, 1)

            project(0, 0)
            project(0, 1)
            k_norms(0)
            for n in range(2, 5):
                project(0, n)
            by_row(obank, 3)
            by_row(ybank, 4)

            def body(i, ffn, attn, pre):
                f = i - 1

                def transpose_h2():
                    wait(pe, s_mod2, 2 * f + 2)
                    wait(pe, s_shared, f)
                    for t in range(NT):
                        ins = pe.transpose(ybank[:, t * P:(t + 1) * P], h2[:, 0, t, 0:P], ident[:, :])
                    ins.then_inc(s_t2, 1)

                def logits():
                    wait(pe, s_h2T, f + 1)
                    wait(pe, s_h2_hi, f + 1)
                    for t in range(NT):
                        ins = pe.matmul(ybank[:, t * NEXP:(t + 1) * NEXP], h2T[:, t * P:(t + 1) * P], rw_sb[:, :],
                                        start=True, stop=True)
                    ins.then_inc(s_logit, 1)

                def transpose_rn():
                    wait(pe, s_rnw, i + 1)
                    wait(pe, s_x2, i)
                    if isinstance(i, int) and i == 0:
                        pe.wait_ge(s_act, 5)
                    for t in range(NT):
                        ins = pe.transpose(at[1][:, t * P:(t + 1) * P],
                                           rn_wide[:, t, :, :].rearrange("p h k -> p (h k)"), ident[:, :])
                    ins.then_inc(s_rnT, 1)

                def spread(v):
                    bank = at[v % 2]
                    if v == 0:
                        wait(pe, s_v_hi, i + 1)
                        wait(pe, s_v_lo, i + 1)
                        wait(pe, s_varc, i)
                    elif v == 1:
                        wait(pe, s_khat, i + 1)
                    else:
                        wait(pe, s_upd, HD * i + v - 1)
                    pe.matmul(bank[:, :], spread_v[:, v, :], vT_hi[:, :], start=True, stop=False)
                    pe.matmul(bank[:, :], spread_v[:, v, :], vT_lo[:, :], start=False, stop=True).then_inc(s_vb, 1)

                def reduce(v):
                    if v == 0:
                        wait(pe, s_og, i)
                        if pre:
                            wait(pe, s_hT, i + 2)
                    if v < HD - 1:
                        wait(pe, s_qS, (HD - 1) * i + v + 1)
                    else:
                        wait(pe, s_q7, i + 1)
                    product = qS[:, v % 2, :] if v < HD - 1 else khat[:, :]
                    pe.matmul(obank[:, :], gather_v[:, v, :], product, start=(v == 0), stop=(v == HD - 1)) \
                        .then_inc(s_red, 1)

                def positions():
                    wait(pe, s_early, (NT + 2) * (f + 1))
                    bank = ybank[:, TB // 2:TB // 2 + NT * NEXP]
                    pe.matmul(bank, before[:, :], both[:, :, :].rearrange("p t e -> p (t e)"), start=True, stop=False)
                    pe.matmul(bank, ones[:, :], earlier[:, 0:NT, :].rearrange("p t e -> p (t e)"),
                              start=False, stop=True).then_inc(s_pos, 1)

                def center_o():
                    wait(pe, s_upd, HD * i + HD - 1)
                    wait(pe, s_og, i + 1)
                    pe.matmul(at[0][:, :], center[:, :], og[:, :], start=True, stop=True).then_inc(s_ctr, 1)

                def variance():
                    wait(pe, s_sq, i + 1)
                    wait(pe, s_oc, i + 1)
                    for t in range(NT):
                        ins = pe.matmul(at[0][:, t:t + 1], oc_sq[:, t * P:(t + 1) * P], mean_col[:, :],
                                        start=True, stop=True)
                    ins.then_inc(s_var, 1)

                def project_out():
                    wait(pe, s_upd, HD * i + HD)
                    for t in range(NT):
                        ins = pe.matmul(at[1][:, t * P:(t + 1) * P], oc[:, t * P:(t + 1) * P], wo_of(i),
                                        start=True, stop=True)
                    ins.then_inc(s_out, 1)

                def wo_of(i):
                    return wo_blk[:, :, :].rearrange("p b n -> p (b n)")[:, bass.ds(i * P, P)]

                def up(e, c):
                    n = NC * e + c
                    if n == 0:
                        wait(pe, s_h2_hi, f + 1)
                        wait(pe, s_h2_lo, f + 1)
                        wait(pe, s_act, 5 * (i + 1) if attn else 5 * NB)
                    wait(pe, s_G, NF1 * f + n - 1)
                    for j in range(2):
                        w = slice(j * HID + c * P, j * HID + (c + 1) * P)
                        ins = split3(ff[2 * c + j][:, :], w13_hi[:, e, w], w13_lo[:, e, w], h2T_hi[:, :], h2T_lo[:, :])
                    ins.then_inc(s_f1, 1)

                def down():
                    wait(pe, s_G, NF1 * (f + 1))
                    wait(pe, s_tgt, TGT_STEPS * f + 1)
                    terms = [(e, c) for e in range(NSH) for c in range(NC)]
                    for t in range(NT):
                        for n, (e, c) in enumerate(terms):
                            ins = pe.matmul(ybank[:, t * P:(t + 1) * P], G[:, NC * e + c, t * P:(t + 1) * P],
                                            w2_sb[:, e, c, :], start=(n == 0), stop=(n == len(terms) - 1))
                    ins.then_inc(s_f2, 1)

                if ffn and isinstance(i, int) and i == 1:
                    pe.wait_ge(s_w13_hi, NFF)
                    pe.wait_ge(s_w13_lo, NFF)
                    pe.wait_ge(ld["w2"], LD["w2"])
                fp = f if ffn else None
                if attn:
                    transpose_rn()
                    spread(0)
                    spread(1)
                    spread(2)
                    spread(3)
                    if not ffn:
                        spread(4)
                    if pre:
                        transpose_x1(i + 1)
                    else:
                        keep_clock(i, 2)
                else:
                    keep_clock(i, 28)
                if ffn:
                    transpose_h2()
                if attn:
                    if ffn:
                        spread(4)
                    reduce(0)
                if ffn:
                    logits()
                if attn:
                    spread(5)
                if ffn and not attn:
                    positions()
                    pe.matmul(at[0][:, 0:NEXP], ones[:, :], earlier[:, NT, :], start=True, stop=True).then_inc(s_total, 1)
                if attn:
                    reduce(1)
                if ffn:
                    up(0, 0)
                if attn:
                    spread(6)
                    reduce(2)
                if ffn:
                    up(0, 1)
                if attn:
                    spread(7)
                    reduce(3)
                    reduce(4)
                if ffn:
                    up(1, 0)
                if attn:
                    reduce(5)
                if ffn and not attn:
                    up(1, 1)
                if attn:
                    reduce(6)
                    reduce(7)
                if pre:
                    project(i + 1, 0, fp)
                if ffn and attn:
                    positions()
                if attn:
                    center_o()
                if ffn and attn:
                    up(1, 1)
                if attn:
                    variance()
                if pre:
                    k_norms(i + 1)
                if attn:
                    project_out()
                if pre:
                    project(i + 1, 1, fp)
                    project(i + 1, 2)
                    project(i + 1, 3)
                    project(i + 1, 4)
                if ffn:
                    down()

            blocks(pe, body)

            pe.wait_ge(s_shared, NB)
            pe.wait_ge(s_table, 1)
            w_hi = w13_hi[:, NSH:, :].rearrange("p e n -> p (e n)")
            w_lo = w13_lo[:, NSH:, :].rearrange("p e n -> p (e n)")
            w_2 = w2_sb[:, NSH:, :, :].rearrange("p e c n -> p (e c n)")
            experts = []

            def rows_T(q, u):
                j = q * U + u
                wait(pe, s_trow[u], 16 * q + 16)
                wait(pe, s_thi, j - 1)
                wait(pe, s_tlo, j - 1)
                pe.transpose(at[u % 2][:, 0:P], rows[:, u, 0:P], ident[:, :]).then_inc(s_tr, 1)

            def first(q, u):
                j = q * U + u
                e = experts[BEHIND_D + u]
                wait(pe, s_thi, j + 1)
                wait(pe, s_tlo, j + 1)
                wait(pe, s_tG, j - 1)
                w = bass.ds(e * 2 * HID, 2 * HID)
                pe.matmul(ff[u % 2][:, :], t_lo[:, u % RING, :], w_hi[:, w], start=True, stop=False)
                pe.matmul(ff[u % 2][:, :], t_hi[:, u % RING, :], w_hi[:, w], start=False, stop=False)
                pe.matmul(ff[u % 2][:, :], t_hi[:, u % RING, :], w_lo[:, w], start=False, stop=True).then_inc(s_tf1, 1)

            def G_T(q, u):
                j = q * U + u
                wait(pe, s_tG, j + 1)
                wait(pe, s_tGT, j - 1)
                for c in range(NC):
                    ins = pe.transpose(ff[2 + u % 2][:, c * P:(c + 1) * P], t_G[:, u % RING, c * P:(c + 1) * P], ident[:, :])
                ins.then_inc(s_tGt, 1)

            def second(q, u, column=None):
                j = q * U + u
                e = experts[BEHIND_D + u - (0 if column is None else column)]
                bank = (ybank, obank)[u % 2]
                wait(pe, s_tGT, j + 1)
                wait(pe, s_ty, j - 1)
                for c in range(NC):
                    ins = pe.matmul(bank[:, 0:P], t_GT[:, u % RING, c * P:(c + 1) * P],
                                    w_2[:, bass.ds(e * HID + c * P, P)], start=(c == 0), stop=(c == NC - 1))
                ins.then_inc(s_tf2, 1)

            def body(q, start, end):
                experts[:] = nc.values_load_multi_w_load_instructions(
                    tile_expert[0:1, bass.ds(q * U, U + BEHIND_D)], engines=(mybir.EngineType.PE,), min_val=0,
                    max_val=NEXP - 1, skip_runtime_bounds_check_because="the table holds minima with NEXP - 1")[1]
                for u in range(U):
                    first(q, u)
                    step(rows_T, q, u, AHEAD, start, end)
                    step(G_T, q, u, -BEHIND_T, start, end)
                    step(lambda q, s: second(q, s, U if s > u else 0), q, u, -BEHIND_D, start, end)
                if end:
                    for n in range(BEHIND_D):
                        if n >= BEHIND_D - BEHIND_T:
                            G_T(q, U - BEHIND_D + n)
                        second(q, U - BEHIND_D + n)

            for u in range(AHEAD):
                rows_T(0, u)
            turns(pe, body)

        @block.scalar
        def _(act):
            act.wait_ge(ld["mod"], LD["mod"])
            act.activation(sc[:, :], c_sb[:, :], ACT.Silu).then_inc(s_sc, 1)

            def normalise_x1(b):
                wait(act, s_t1, b)
                for t in range(NT):
                    col = b * NT + t
                    ins = act.activation(xn1[:, t, :], xall[:, :, :].rearrange("p n d -> p (n d)")[:, bass.ds(col * P, P)],
                                         ACT.Identity, bias=nmr1[:, bass.ds(col, 1)], scale=rstd1[:, bass.ds(col, 1)])
                ins.then_inc(s_xn1, 1)

            def modulate_1(b):
                wait(act, s_t1, b + 1)
                wait(act, s_hT_lo, b)
                bank = at[0] if isinstance(b, int) and b == 0 else obank
                act.activation(hT[:, :], bank[:, :], ACT.Identity, bias=shift1[:, bass.ds(b, 1)],
                               scale=scale1[:, bass.ds(b, 1)]).then_inc(s_hT, 1)
                wait(act, s_hT, b + 1)
                wait(act, s_proj, 5 * b)
                act.activation(hT_hi[:, :], hT[:, :], ACT.Copy).then_inc(s_hT_hi, 1)

            act.wait_ge(s_st1, 1)
            normalise_x1(0)
            act.wait_ge(s_watt, 1)
            act.activation(watt_hi[:, :, :], watt[:, :, :], ACT.Copy).then_inc(s_watt_hi, 1)
            act.wait_ge(s_ready, 1)
            modulate_1(0)
            def activate(b, n, dst, func, scale=1.0):
                wait(act, s_proj, 5 * b + n + 1)
                act.activation(dst[:, :], bank_of(b, n)[:, :], func, scale=scale).then_inc(s_act, 1)

            def take_k(b):
                wait(act, s_khat, b)
                activate(b, 0, kT, ACT.Silu)
                wait(act, s_n2, b)
                wait(act, s_act, 5 * b + 1)
                act.activation(ksq[:, :], kT[:, :], ACT.Square).then_inc(s_ksq, 1)

            def take_projections(b):
                wait(act, s_scan, HD * b)
                activate(b, 1, decay, ACT.Tanh, 0.5)
                wait(act, s_v_lo, b)
                activate(b, 2, vT, ACT.Silu)
                wait(act, s_og, b)
                activate(b, 3, gate, ACT.Tanh, 0.5)
                wait(act, s_vb, HD * b)
                wait(act, s_act, 5 * b + 3)
                act.activation(vT_hi[:, :], vT[:, :], ACT.Copy).then_inc(s_v_hi, 1)
                wait(act, s_qS, (HD - 1) * b)
                wait(act, s_q7, b)
                activate(b, 4, qT, ACT.Silu)
                act.activation(decay[:, :], decay[:, :], ACT.Copy, bias=0.5, scale=0.5).then_inc(s_decay, 1)
                wait(act, s_act, 5 * b + 4)
                act.activation(gate[:, :], gate[:, :], ACT.Copy, bias=0.5, scale=0.5).then_inc(s_gate, 1)

            take_k(0)
            take_projections(0)
            act.wait_ge(s_rows, 4)
            for bank, dst, one in ((ybank, scale2_row, 1.0), (obank, shift2_row, 0.0)):
                for k in range(BPB):
                    ins = act.activation(dst[:, :, :].rearrange("p (b k) n -> p b k n", k=BPB)[:, :, k, :],
                                         bank[:, :].rearrange("p (b n) -> p b n", n=P), ACT.Copy, bias=one)
            ins.then_inc(s_row2, 1)
            def body(i, ffn, attn, pre):
                f = i - 1

                def silu_chunk(e, c):
                    n = NC * e + c
                    wait(act, s_G, NF1 * f + n - 1)
                    wait(act, s_f1, NF1 * f + n + 1)
                    act.activation(silu[:, c, :], ff[2 * c][:, :], ACT.Silu).then_inc(s_silu, 1)

                if pre:
                    if isinstance(i, int) and i <= 1:
                        act.wait_ge(s_st1, i + 2)
                    normalise_x1(i + 1)
                    modulate_1(i + 1)
                if isinstance(i, int) and i == 0:
                    act.wait_ge(ld["w13"], LD["w13"])
                    for e in range(NFF):
                        act.activation(w13_hi[:, e, :], w13[:, e, :], ACT.Copy).then_inc(s_w13_hi, 1)
                    act.wait_ge(s_gains, 1)
                    for k in range(BPB):
                        ins = act.activation(gain_b[:, :, :].rearrange("p (b k) n -> p b k n", k=BPB)[:, :, k, :],
                                             gain_b1[:, :, :], ACT.Copy)
                    ins.then_inc(s_gain_b, 1)
                if ffn:
                    wait(act, s_t2, f + 1)
                    wait(act, s_f1, NF1 * f)
                    wait(act, s_logit, f)
                    wait(act, s_h2_lo, f)
                    act.activation(h2T[:, :], ybank[:, :], ACT.Copy).then_inc(s_h2T, 1)
                    act.activation(h2T_hi[:, :], ybank[:, :], ACT.Copy).then_inc(s_h2_hi, 1)
                if ffn:
                    wait(act, s_scatter, 16 * 2 * NT * f)
                    act.activation(h2[:, 1, :, 0:P], h2[:, 0, :, 0:P], ACT.Copy).then_inc(s_copy2, 1)
                    silu_chunk(0, 0)
                    silu_chunk(0, 1)
                    wait(act, s_dif, f + 1)
                    wait(act, s_wt, f)
                    act.activation(tanh_d[:, :], dif[:, :], ACT.Tanh, scale=0.5).then_inc(s_tanh, 1)
                    silu_chunk(1, 0)
                    if not attn:
                        silu_chunk(1, 1)
                if pre:
                    take_k(i + 1)
                if attn:
                    wait(act, s_ctr, i + 1)
                    wait(act, s_var, i)
                    act.activation(oc_sq[:, :], at[0][:, :], ACT.Square).then_inc(s_sq, 1)
                    wait(act, s_out, i)
                    act.activation(oc[:, :], at[0][:, :], ACT.Copy).then_inc(s_oc, 1)
                    if ffn:
                        silu_chunk(1, 1)
                if pre:
                    take_projections(i + 1)
                if attn:
                    wait(act, s_st2, i + 1)
                    wait(act, s_mod2, 2 * i)
                    for t in range(NT):
                        ins = act.activation(xn2[:, t, :],
                                             xall[:, :, :].rearrange("p n d -> p (n d)")[:, bass.ds((i * NT + t) * P, P)],
                                             ACT.Identity, bias=nmr2[:, t:t + 1], scale=rstd2[:, t:t + 1])
                    ins.then_inc(s_xn2, 1)
                if ffn:
                    wait(act, s_f2, f + 1)
                    wait(act, s_xsh, f)
                    act.activation(shared[:, :, :], ybank[:, :].rearrange("p (t n) -> p t n", n=P), ACT.Copy) \
                        .then_inc(s_shared, 1)

            blocks(act, body)

            def hi(q, u):
                j = q * U + u
                wait(act, s_tr, j + 1)
                wait(act, s_tf1, j - RING + 1)
                act.activation(t_hi[:, u % RING, :], at[u % 2][:, 0:P], ACT.Copy).then_inc(s_thi, 1)

            def silu_rows(q, u):
                j = q * U + u
                wait(act, s_tf1, j + 1)
                wait(act, s_tG, j - 1)
                act.activation(t_silu[:, u % 2, :], ff[u % 2][:, 0:HID], ACT.Silu).then_inc(s_tsilu, 1)

            def take_y(q, u):
                j = q * U + u
                wait(act, s_tf2, j + 1)
                wait(act, s_yrow[u], 16 * q)
                act.activation(y_sb[:, u, :], (ybank, obank)[u % 2][:, 0:P], ACT.Copy).then_inc(s_ty, 1)

            def body(q, start, end):
                for u in range(U):
                    silu_rows(q, u)
                    step(hi, q, u, AHEAD, start, end)
                    step(take_y, q, u, -BEHIND_D, start, end)
                if end:
                    for n in range(BEHIND_D):
                        take_y(q, U - BEHIND_D + n)

            for u in range(AHEAD):
                hi(0, u)
            turns(act, body)

            def body(m):
                for u in range(V):
                    wait(act, s_yin[u], 32 * m + 32)
                    wait(act, s_out3, V * m + u + 1 - V)
                    for t in range(NT):
                        ins = act.activation(total[:, u, t * P:(t + 1) * P], y_in[:, u, 0, t * P:(t + 1) * P], ACT.Copy,
                                             scale=wt[:, 0, bass.ds((V * m + u) * NT + t, 1)])
                    ins.then_inc(s_part, 1)

            groups(act, body)

        @block.gpsimd
        def _(pool):
            def split_h(b):
                wait(pool, s_hT_hi, b + 1)
                wait(pool, s_proj, 5 * b)
                pool.tensor_tensor(hT_lo[:, :], hT[:, :], hT_hi[:, :].bitcast(F32), ALU.subtract).then_inc(s_hT_lo, 1)

            def split_v(b):
                wait(pool, s_vb, HD * b)
                wait(pool, s_v_hi, b + 1)
                pool.tensor_tensor(vT_lo[:, :], vT[:, :], vT_hi[:, :].bitcast(F32), ALU.subtract).then_inc(s_v_lo, 1)

            def add_shared(f):
                g = gain_b[:, :, :].rearrange("p b n -> p (b n)")[:, bass.ds(f * P, P)].unsqueeze(1) \
                    .broadcast_to([P, NT, P])
                if isinstance(f, int) and f == 0:
                    pool.wait_ge(s_gain_b, 1)
                wait(pool, s_shared, f + 1)
                pool.tensor_tensor(shared[:, :, :], shared[:, :, :], g, ALU.mult).then_inc(s_shg, 1)
                wait(pool, s_shg, f + 1)
                x_f = xall[:, bass.ds(f * NT, NT), :]
                pool.tensor_tensor(x_f, x_f, shared[:, :, :], ALU.add).then_inc(s_xsh, 1)

            split_h(0)
            split_v(0)

            def body(i, ffn, attn, pre):
                f = i - 1

                def query(v):
                    wait(pool, s_scan, HD * i + v + 1)
                    wait(pool, s_red, HD * i + v - 1)
                    pool.tensor_tensor(qS[:, v % 2, :], S[:, v, :], qT[:, :], ALU.mult).then_inc(s_qS, 1)

                for v in range(HD - 1):
                    if attn:
                        query(v)
                    if v == 1 and ffn:
                        wait(pool, s_f1, NF1 * f)
                        wait(pool, s_h2_hi, f + 1)
                        pool.tensor_tensor(h2T_lo[:, :], h2T[:, :], h2T_hi[:, :].bitcast(F32), ALU.subtract) \
                            .then_inc(s_h2_lo, 1)
                    if v == 3 and pre:
                        split_h(i + 1)
                if isinstance(i, int) and i == 0:
                    for e in range(NFF):
                        pool.wait_ge(s_w13_hi, e + 1)
                        pool.tensor_tensor(w13_lo[:, e, :], w13[:, e, :], w13_hi[:, e, :].bitcast(F32), ALU.subtract) \
                            .then_inc(s_w13_lo, 1)
                if ffn:
                    if not (isinstance(i, int) and i == 1):
                        add_shared(f - 1)
                    wait(pool, s_car, f)
                    wait(pool, s_target, f + 1)
                    wait(pool, s_copy2, f + 1)
                    wait(pool, s_ids, f + 1)
                    pool.tensor_tensor(carrier[:, 2:3], keep[:, 0:1], keep[:, 0:1], ALU.mult).then_inc(s_car, 1)
                    for k in range(2):
                        for t in range(NT):
                            pool.indirect_dma_start(
                                out=h_dram[:, :], out_offset=bass.IndirectOffsetOnAxis(ap=target_i[:, k, t:t + 1], axis=0),
                                in_=h2[:, k, t, :], in_offset=None).then_inc(s_scatter, 16)
                if pre:
                    split_v(i + 1)
                if attn:
                    def row(buffer):
                        return buffer[:, :, :].rearrange("p b n -> p (b n)")[:, bass.ds(i * P, P)].unsqueeze(1) \
                            .broadcast_to([P, NT, P])

                    if isinstance(i, int) and i == 0:
                        pool.wait_ge(s_row2, 1)
                    wait(pool, s_xn2, i + 1)
                    wait(pool, s_scatter, 16 * 2 * NT * i)
                    wait(pool, s_copy2, i)
                    pool.tensor_tensor(h2[:, 0, :, 0:P], xn2[:, :, :], row(scale2_row), ALU.mult).then_inc(s_mod2, 1)
                    wait(pool, s_mod2, 2 * i + 1)
                    pool.tensor_tensor(h2[:, 0, :, 0:P], h2[:, 0, :, 0:P], row(shift2_row), ALU.add).then_inc(s_mod2, 1)

            blocks(pool, body)
            add_shared(NB - 1)

            def body(q, start, end):
                for u in range(U):
                    j = q * U + u
                    wait(pool, s_tcar, j)
                    wait(pool, s_ty, j + 1)
                    wait(pool, s_trow[u], 16 * q + 16)
                    pool.tensor_tensor(carrier[:, 3:4], keep[:, 0:1], keep[:, 0:1], ALU.mult).then_inc(s_tcar, 1)
                    pool.indirect_dma_start(
                        out=y_dram[:, :], out_offset=bass.IndirectOffsetOnAxis(ap=rows[:, u, P:P + 1].bitcast(I32), axis=0),
                        in_=y_sb[:, u, :], in_offset=None).then_inc(s_yrow[u], 16)

            turns(pool, body)

            def body(m):
                for u in range(V):
                    wait(pool, s_sum, V * m + u + 1)
                    g = gain_b[:, :, :].rearrange("p b n -> p (b n)")[:, bass.ds((V * m + u) * P, P)].unsqueeze(1) \
                        .broadcast_to([P, NT, P])
                    tot = total[:, u, :].rearrange("p (t n) -> p t n", n=P)
                    pool.tensor_tensor(tot, tot, g, ALU.mult).then_inc(s_fin, 1)

            groups(pool, body)

        @block.vector
        def _(dve):
            link = Chain(dve, s_set, 0)

            def raw_statistics(a, b):
                for t in range(a, b):
                    ins = dve.bn_stats(bn[:, t, :], xall[:, t, :])
                link(ins)

            def statistics_1(a, b):
                for t in range(a, b):
                    ins = dve.bn_aggr(mv[:, t, :], bn[:, t, :])
                link(ins)
                link(dve.tensor_scalar(var1[:, a:b], mv[:, a:b, 1], 1e-5, None, ALU.add))
                rsqrt(dve, link, rstd1[:, a:b], var1[:, a:b], tmp1[:, a:b])
                dve.scalar_tensor_tensor(nmr1[:, a:b], mv[:, a:b, 0], -1.0, rstd1[:, a:b], ALU.mult, ALU.mult) \
                    .then_inc(s_st1, 1)

            dve.wait_ge(s_sc, 1)
            dve.tensor_copy(sc_wide[:, :, :], sc[:, :].unsqueeze(2).broadcast_to([P, B, P])).then_inc(s_scw, 1)
            dve.wait_ge(ld["x0"], LD["x0"])
            raw_statistics(0, NT)
            statistics_1(0, NT)
            dve.wait_ge(ld["attw"], LD["attw"])
            dve.tensor_copy(watt[:, 0:3, :].rearrange("p w n -> p (w n)"), wqkv_sb)
            dve.tensor_copy(watt[:, 3, :].rearrange("p (h k) -> p h k", k=HD), wf_sb[:, :].unsqueeze(2).broadcast_to([P, H, HD]))
            dve.wait_ge(s_mod, 1)
            link(dve.tensor_copy(watt[:, 4, :], ff[3][:, 0:P]))
            dve.nop().then_inc(s_watt, 1)
            m = ff[0]
            for n, dst, one in ((0, shift1, 0.0), (1, scale1, 1.0), (2, shift2, 0.0), (3, scale2, 1.0)):
                ins = dve.tensor_scalar(dst[:, :].rearrange("p (b k) -> p b k", k=BPB),
                                        m[:, n * B:(n + 1) * B].unsqueeze(2).broadcast_to([P, B, BPB]), one, None, ALU.add)
            ins.then_inc(s_ready, 1)
            dve.wait_ge(s_watt_hi, 1)
            dve.tensor_tensor(watt_lo[:, :, :], watt[:, :, :], watt_hi[:, :, :].bitcast(F32), ALU.subtract) \
                .then_inc(s_watt_lo, 1)
            dve.wait_ge(ld["consts"], LD["consts"])
            dve.tensor_copy(spread_v[:, :, :].rearrange("p v (h k) -> p v h k", k=HD),
                            ident[:, :].rearrange("p (h v) -> p v h", v=HD).unsqueeze(3).broadcast_to([P, HD, H, HD]))
            link(dve.memset(gather_v[:, :, :], 0.0))
            for v in range(HD):
                dve.tensor_copy(gather_v[:, v, :].rearrange("p (h k) -> p h k", k=HD)[:, :, v],
                                gather_src(block_diag, ident, v, H, HD))
            dve.memset(S[:, :, TB - 1], 0.0)
            dve.memset(earlier[:, NT, :], 0.0)
            link(dve.memset(tile_expert[:, :], 0))

            dve.wait_ge(ld["x1"], LD["x1"])
            raw_statistics(NT, 2 * NT)
            statistics_1(NT, 2 * NT)

            def gains(n, dst):
                g = ff[1 + n][:, :].rearrange("p (b n) -> p b n", n=P)
                dve.wait_ge(s_rows, n + 1)
                dve.tensor_scalar(gsign[:, :, :], g, 0.0, 2.0, ALU.is_ge, ALU.mult)
                link(dve.tensor_scalar(gabs[:, :, :], g, -1.0, 0.25, ALU.mult, ALU.max))
                link(dve.tensor_tensor(gabs[:, :, :], gabs[:, :, :], g, ALU.max))
                link(dve.scalar_tensor_tensor(dst[:, :, :], gsign[:, :, :], -1.0, gabs[:, :, :], ALU.add, ALU.mult))

            def fold_gain_a():
                link(dve.tensor_scalar(wo_ln[:, :], wo_sb[:, :], lnw_sb[:, 0:1], None, ALU.mult))
                for k in range(BPB):
                    ins = dve.tensor_tensor(wo_blk[:, :, :].rearrange("p (b k) n -> p b k n", k=BPB)[:, :, k, :],
                                            gain_a[:, :, :], wo_ln[:, :].unsqueeze(1).broadcast_to([P, B, P]), ALU.mult)
                link(ins)

            def table_of_tiles():
                link = Chain(dve, s_tab, 0)
                dve.wait_ge(s_total, 1)
                link(dve.tensor_copy(counts[:, :], at[0][0:1, 0:NEXP]))
                link(dve.tensor_tensor(pad_row[:, :], counts[:, :], region[0:1, :], ALU.add))
                dve.nop().then_inc(s_prow, 1)
                link(dve.tensor_scalar(ntiles_i[:, :], counts[:, :], float(P - 1), None, ALU.add))
                link(dve.tensor_scalar(ntiles_i[:, :], ntiles_i[:, :], P.bit_length() - 1, None, ALU.logical_shift_right))
                link(dve.tensor_copy(ntiles[:, :], ntiles_i[:, :]))
                link(dve.tensor_tensor_scan(last[:, :], one_row, ntiles[:, :], 0.0, ALU.mult, ALU.add))
                link(dve.tensor_scalar(jump[:, :], ntiles[:, :], float(-P), float(REG), ALU.mult, ALU.add))
                table = [1, NTILE, NEXP]
                link(dve.tensor_tensor(past[:, :, :], tile_no.unsqueeze(2).broadcast_to(table),
                                       last[:, :].unsqueeze(1).broadcast_to(table), ALU.is_ge))
                link(dve.tensor_tensor(skip[:, :, :], past[:, :, :], jump[:, :].unsqueeze(1).broadcast_to(table), ALU.mult))
                link(dve.tensor_reduce(tile_sum[:, 0, :], past[:, :, :], AX.X, ALU.add))
                link(dve.tensor_reduce(tile_sum[:, 1, :], skip[:, :, :], AX.X, ALU.add))
                link(dve.tensor_scalar(tile_expert[:, BEHIND_D:], tile_sum[:, 0, :], float(NEXP - 1), None, ALU.min))
                link(dve.scalar_tensor_tensor(tile_row[:, :], tile_no, float(P), tile_sum[:, 1, :], ALU.mult, ALU.add))
                dve.nop().then_inc(s_table, 1)

            def take_norms(b):
                wait(dve, s_n2, b + 1)
                return dve.tensor_scalar(n2, norm_bank(b)[:, 0:NT * H], 1e-24, None, ALU.max)

            def widen_norms(b):
                wait(dve, s_rnT, b)
                dve.tensor_copy(rn_wide[:, :, :, :], rn.rearrange("p (t h) -> p t h", h=H).unsqueeze(3)
                                .broadcast_to([P, NT, H, HD])).then_inc(s_rnw, 1)

            norm_link = Chain(dve, s_norm, 0)
            norm_link(take_norms(0))
            rsqrt(dve, norm_link, rn, n2, rtmp[:, 0:NT * H])
            widen_norms(0)

            def body(i, ffn, attn, pre):
                f = i - 1

                def product(e, c):
                    n = NC * e + c
                    wait(dve, s_f2, f)
                    wait(dve, s_silu, NF1 * f + n + 1)
                    dve.tensor_tensor(G[:, n, :], ff[2 * c + 1][:, :], silu[:, c, :], ALU.mult).then_inc(s_G, 1)

                wide = [P, NT, NEXP]

                def choose():
                    link = Chain(dve, s_rt, RT_STEPS * f)
                    wait(dve, s_logit, f + 1)
                    wait(dve, s_tgt, TGT_STEPS * f)
                    link(dve.tensor_tensor(lg[:, :, :], ybank[:, 0:NT * NEXP].rearrange("p (t e) -> p t e", e=NEXP),
                                           bias_sb[:, :].unsqueeze(1).broadcast_to(wide), ALU.add))
                    dve.memset(carrier[:, 4:5], 0.0)
                    for t in range(NT):
                        ins = dve.max(top[:, t, :], lg[:, t, :])
                    link(ins)
                    pair = [P, 2, NT, NEXP]
                    link(dve.tensor_tensor(eq[:, :, :, :], lg[:, :, :].unsqueeze(1).broadcast_to(pair),
                                           top[:, :, 0:2].rearrange("p t k -> p k t").unsqueeze(3).broadcast_to(pair), ALU.is_equal))
                    link(dve.tensor_tensor(eq[:, :, :, :], eq[:, :, :, :],
                                           rank[:, :].unsqueeze(1).unsqueeze(1).broadcast_to(pair), ALU.mult))

                    def highest(k):
                        link(dve.tensor_reduce(r[:, k, :], eq[:, k, :, :], AX.X, ALU.max))
                        link(dve.tensor_tensor(hot[:, k, :, :], eq[:, k, :, :], r[:, k, :].unsqueeze(2).broadcast_to(wide),
                                               ALU.is_equal))

                    highest(0)
                    link(dve.scalar_tensor_tensor(eq[:, 1, :, :], hot[:, 0, :, :], -2.0 * NEXP, eq[:, 1, :, :], ALU.mult, ALU.add))
                    highest(1)
                    assert link.n == RT_STEPS
                    wait(dve, s_tanh, f)
                    dve.tensor_tensor(dif[:, :], top[:, :, 0], top[:, :, 1], ALU.subtract).then_inc(s_dif, 1)

                def count():
                    wait(dve, s_pos, f)
                    wait(dve, s_rt, RT_STEPS * (f + 1))
                    link = Chain(dve, s_early, (NT + 2) * f)
                    link(dve.tensor_tensor(both[:, :, :], hot[:, 0, :, :], hot[:, 1, :, :], ALU.add))
                    link(dve.tensor_copy(earlier[:, 0, :], earlier[:, NT, :]))
                    for t in range(NT):
                        link(dve.tensor_tensor(earlier[:, t + 1, :], earlier[:, t, :], both[:, t, :], ALU.add))

                def weigh():
                    wait(dve, s_tanh, f + 1)
                    for k, sign in enumerate((0.5, -0.5)):
                        ins = dve.tensor_scalar(wt[:, k, bass.ds(f * NT, NT)], tanh_d[:, :], sign, 0.5, ALU.mult, ALU.add)
                    ins.then_inc(s_wt, 1)

                def targets():
                    link = Chain(dve, s_tgt, TGT_STEPS * f)
                    wait(dve, s_pos, f + 1)
                    link(dve.tensor_tensor(place[:, :, :], ybank[:, TB // 2:TB // 2 + NT * NEXP]
                                           .rearrange("p (t e) -> p t e", e=NEXP),
                                           region[:, :].unsqueeze(1).broadcast_to(wide), ALU.add))
                    link(dve.tensor_tensor(chosen[:, :, :, :], hot[:, :, :, :],
                                           place[:, :, :].unsqueeze(1).broadcast_to([P, 2, NT, NEXP]), ALU.mult))
                    link(dve.tensor_reduce(target[:, :, :], chosen[:, :, :, :], AX.X, ALU.add))
                    wait(dve, s_scatter, 16 * 2 * NT * f)
                    link(dve.tensor_copy(target_i[:, :, :], target[:, :, :]))
                    assert link.n == TGT_STEPS
                    dve.nop().then_inc(s_target, 1)
                    own = ids_sb[:, :, bass.ds(f * NT, NT)]
                    dve.tensor_tensor(h2[:, :, :, P].bitcast(I32), own, own, ALU.max).then_inc(s_ids, 1)

                def start_state():
                    wait(dve, s_qS, (HD - 1) * i)
                    wait(dve, s_scan, HD * i)
                    dve.tensor_scalar(S0[:, :], S[:, :, TB - 1], keep[:, bass.ds(i, 1)], None, ALU.mult).then_inc(s_S0, 1)

                def normalise_k():
                    wait(dve, s_rnT, i + 1)
                    wait(dve, s_upd, HD * i)
                    dve.tensor_tensor(khat[:, :], at[1][:, :], kT[:, :], ALU.mult).then_inc(s_khat, 1)

                def update(v):
                    if v == 0:
                        wait(dve, s_khat, i + 1)
                    wait(dve, s_vb, HD * i + v + 1)
                    wait(dve, s_scan, HD * i + v - 2)
                    dve.tensor_tensor(upd[:, v % 3, :], at[v % 2][:, :], khat[:, :], ALU.mult).then_inc(s_upd, 1)

                def scan(v):
                    if v == 0:
                        wait(dve, s_decay, i + 1)
                        wait(dve, s_S0, i + 1)
                    wait(dve, s_upd, HD * i + v + 1)
                    dve.tensor_tensor_scan(S[:, v, :], decay[:, :], upd[:, v % 3, :], S0[:, v:v + 1], ALU.mult, ALU.add) \
                        .then_inc(s_scan, 1)

                def last_query():
                    wait(dve, s_upd, HD * i + HD)
                    wait(dve, s_scan, HD * i + HD)
                    dve.tensor_tensor(khat[:, :], S[:, HD - 1, :], qT[:, :], ALU.mult).then_inc(s_q7, 1)

                def gate_o():
                    wait(dve, s_red, HD * i + HD)
                    wait(dve, s_gate, i + 1)
                    wait(dve, s_ctr, i)
                    dve.tensor_tensor(og[:, :], obank[:, :], gate[:, :], ALU.mult).then_inc(s_og, 1)

                def residual():
                    link = Chain(dve, s_ln, RSQRT_STEPS * i)
                    wait(dve, s_var, i + 1)
                    if pre:
                        take_norms(i + 1)
                    dve.tensor_scalar(ovar, at[0][:, 0:NT], 1e-5, None, ALU.add).then_inc(s_varc, 1)
                    dve.wait_ge(s_varc, i + 1)
                    rsqrt(dve, link, rsq[:, :], sq[:, :], rtmp[:, :])
                    wait(dve, s_out, i + 1)
                    flat = xall[:, :, :].rearrange("p n d -> p (n d)")
                    for t in range(NT):
                        xt = flat[:, bass.ds((i * NT + t) * P, P)]
                        ins = dve.scalar_tensor_tensor(xt, at[1][:, t * P:(t + 1) * P], orstd[:, t:t + 1], xt,
                                                       ALU.mult, ALU.add)
                    ins.then_inc(s_x2, 1)
                    if pre:
                        widen_norms(i + 1)
                    dve.wait_ge(s_x2, i + 1)
                    wait(dve, s_xn2, i)
                    dve.memset(carrier[:, 0:1], 0.0)
                    link = Chain(dve, s_st, (RSQRT_STEPS + 3) * i)
                    for t in range(NT):
                        ins = dve.bn_stats(bn2[:, t, :], flat[:, bass.ds((i * NT + t) * P, P)])
                    link(ins)
                    dve.memset(carrier[:, 1:2], 0.0)
                    for t in range(NT):
                        ins = dve.bn_aggr(mv2[:, t, :], bn2[:, t, :])
                    link(ins)
                    link(dve.tensor_scalar(var2[:, :], mv2[:, :, 1], 1e-5, None, ALU.add))
                    rsqrt(dve, link, rstd2[:, :], var2[:, :], tmp2[:, :])
                    dve.scalar_tensor_tensor(nmr2[:, :], mv2[:, :, 0], -1.0, rstd2[:, :], ALU.mult, ALU.mult) \
                        .then_inc(s_st2, 1)

                start = isinstance(i, int) and i == 0
                if attn:
                    start_state()
                    normalise_k()
                    update(0)
                    update(1)
                    scan(0)
                    update(2)
                    scan(1)
                    if start:
                        gains(0, gain_a)
                    update(3)
                    scan(2)
                    if start:
                        gains(1, gain_b1)
                        dve.nop().then_inc(s_gains, 1)
                    update(4)
                    scan(3)
                if start:
                    fold_gain_a()
                    dve.wait_ge(ld["xrest"], LD["xrest"])
                    dve.wait_ge(ld["table"], LD["table"])
                    raw_statistics(2 * NT, 3 * NT)
                if ffn:
                    choose()
                if ffn and not attn:
                    count()
                    targets()
                    table_of_tiles()
                if attn:
                    update(5)
                    scan(4)
                if ffn:
                    product(0, 0)
                if attn:
                    update(6)
                    scan(5)
                if ffn:
                    product(0, 1)
                if start:
                    raw_statistics(3 * NT, 5 * NT)
                if attn:
                    update(7)
                    scan(6)
                    scan(7)
                    last_query()
                if start:
                    raw_statistics(5 * NT, NB * NT)
                if ffn:
                    product(1, 0)
                if ffn and attn:
                    count()
                if attn:
                    gate_o()
                if ffn:
                    weigh()
                if ffn and attn:
                    targets()
                if ffn:
                    product(1, 1)
                if start:
                    statistics_1(2 * NT, NB * NT)
                if attn:
                    residual()

            blocks(dve, body)

            def lo(q, u):
                j = q * U + u
                wait(dve, s_thi, j + 1)
                wait(dve, s_tf1, j - RING + 1)
                dve.tensor_tensor(t_lo[:, u % RING, :], at[u % 2][:, 0:P], t_hi[:, u % RING, :].bitcast(F32), ALU.subtract) \
                    .then_inc(s_tlo, 1)

            def gated(q, u):
                j = q * U + u
                wait(dve, s_tsilu, j + 1)
                wait(dve, s_tGt, j - RING + 1)
                dve.tensor_tensor(t_G[:, u % RING, :], ff[u % 2][:, HID:2 * HID], t_silu[:, u % 2, :], ALU.mult) \
                    .then_inc(s_tG, 1)

            def take_GT(q, u):
                j = q * U + u
                wait(dve, s_tGt, j + 1)
                wait(dve, s_tf2, j - RING + 1)
                dve.tensor_copy(t_GT[:, u % RING, :], ff[2 + u % 2][:, 0:HID]).then_inc(s_tGT, 1)

            def body(q, start, end):
                for u in range(U):
                    step(take_GT, q, u, -BEHIND_T, start, end)
                    gated(q, u)
                    step(lo, q, u, AHEAD, start, end)
                if end:
                    for n in range(BEHIND_T):
                        take_GT(q, U - BEHIND_T + n)

            for u in range(AHEAD):
                lo(0, u)
            turns(dve, body)

            def body(m):
                def add_second(u):
                    wait(dve, s_part, V * m + u + 1)
                    for t in range(NT):
                        c = slice(t * P, (t + 1) * P)
                        ins = dve.scalar_tensor_tensor(total[:, u, c], y_in[:, u, 1, c], wt[:, 1, bass.ds((V * m + u) * NT + t, 1)],
                                                       total[:, u, c], ALU.mult, ALU.add)
                    ins.then_inc(s_sum, 1)

                def add_x(u):
                    wait(dve, s_fin, V * m + u + 1)
                    wait(dve, s_store[u], 16 * m)
                    tot, dst = (a[:, u, :].rearrange("p (t n) -> p t n", n=P) for a in (total, res))
                    dve.tensor_tensor(dst, tot, xall[:, bass.ds((V * m + u) * NT, NT), :], ALU.add).then_inc(s_out3, 1)

                for u in range(V + 1):
                    if u < V:
                        add_second(u)
                    if u >= 1:
                        add_x(u - 1)

            groups(dve, body)


def gather_src(block_diag, ident, v, H, HD):
    return block_diag[:, :].rearrange("p (h k) -> p h k", k=HD)[:, :, v]


def constants(H, HD, NEXP, NB, BPB):
    import numpy as np

    p = np.arange(P)
    parts = [
        np.eye(P),
        p[:, None] // HD == np.arange(H)[None, :],
        p[:, None] // HD == p[None, :] // HD,
        np.eye(P) - 1.0 / P,
        p[:, None] < p[None, :],
        np.ones((P, P)),
        np.full((P, 1), 1.0 / P),
        np.broadcast_to(NEXP - np.arange(NEXP), (P, NEXP)),
        np.broadcast_to(np.arange(NB) % BPB != 0, (P, NB)),
        np.broadcast_to(np.arange(NEXP) * (NB * TB + P), (P, NEXP)),
    ]
    return np.concatenate([np.asarray(a, np.float32) for a in parts], axis=1)


def tables(NTOK, NEXP):
    import numpy as np

    tile = np.arange(NTOK // P)
    ids = np.arange(P)[:, None, None] + tile[None, None, :] * P + np.array([0, NTOK])[None, :, None]
    full = 2 * NTOK // P
    ntile = -(-(full + NEXP - 1) // U) * U
    pads = np.zeros((NEXP + ntile - full, P, P + 1), np.float32)
    pads[:, :, P] = (2 * NTOK + np.arange(pads.shape[0] * P, dtype=np.int32)).reshape(-1, P).view(np.float32)
    row = np.concatenate([np.arange(ntile), np.ones(NEXP)]).astype(np.float32).reshape(1, -1)
    return ids.astype(np.int32), row, pads


def kernel(L0_attn_x, L0_attn_Wq, L0_attn_Wk, L0_attn_Wv, L0_attn_Wf, L0_attn_Wg1, L0_attn_Wg2, L0_attn_ln_w,
           L0_attn_Wo, L0_ffn_router_w, L0_ffn_expert_bias, L0_ffn_w1, L0_ffn_w3, L0_ffn_w2, L0_ffn_sw1, L0_ffn_sw3,
           L0_ffn_sw2, L0_c, L0_wmod):
    import numpy as np
    import concourse.bacc as bacc
    from concourse.bass_utils import run_bass_kernel_spmd

    x = np.asarray(L0_attn_x)
    B, N, D = x.shape
    H = L0_attn_Wf.shape[0]
    NEXP, HID = L0_ffn_w1.shape[:2]
    NC = HID // P
    w1 = np.concatenate([np.asarray(L0_ffn_sw1), np.asarray(L0_ffn_w1)])
    w3 = np.concatenate([np.asarray(L0_ffn_sw3), np.asarray(L0_ffn_w3)])
    w2 = np.concatenate([np.asarray(L0_ffn_sw2), np.asarray(L0_ffn_w2)])
    NFF = w1.shape[0]
    w13 = np.stack([w1, w3], axis=1)
    ids, tiles, pads = tables(B * N, NEXP)
    arrays = {
        "x": x,
        "cmod": np.concatenate([np.asarray(L0_c).T, np.asarray(L0_wmod)], axis=1),
        "attw": np.concatenate([np.asarray(w).T for w in (L0_attn_Wq, L0_attn_Wk, L0_attn_Wv, L0_attn_Wf, L0_attn_Wo)]
                               + [np.asarray(L0_attn_ln_w).reshape(D, 1), np.asarray(L0_ffn_router_w).T], axis=1),
        "wg12": np.concatenate([np.asarray(L0_attn_Wg1), np.asarray(L0_attn_Wg2).T], axis=1),
        "w13T": w13.transpose(3, 0, 1, 2).reshape(D, NFF, 2 * HID),
        "w2T": w2.reshape(NFF, D, NC, P).transpose(3, 0, 2, 1),
        "bias": np.asarray(L0_ffn_expert_bias),
        "consts": constants(H, D // H, NEXP, B * N // TB, N // TB),
        "ids": ids,
        "tiles": tiles,
        "pads": pads,
    }
    nc = bacc.Bacc("TRN2", target_bir_lowering=False, num_devices=1)
    in_map, args = {}, []
    for name, a in arrays.items():
        a = np.ascontiguousarray(a)
        in_map[f"in_{name}"] = a
        args.append(nc.dram_tensor(f"in_{name}", a.shape, mybir.dt.from_np(a.dtype), kind="ExternalInput").ap())
    args.append(H)
    args.append(nc.dram_tensor("out_0", x.shape, mybir.dt.from_np(x.dtype), kind="ExternalOutput").ap())
    build(nc, *args)
    r = run_bass_kernel_spmd(nc, [in_map], core_ids=[0])
    return r.results[0]["out_0"]
```
